# Optimizing a Trainium2 kernel written in Bass

```python
import numpy as np
import jax
import jax.numpy as jnp

def _softmax(x, axis=-1):
    return jax.nn.softmax(x, axis=axis)

def _gelu(x):
    return jax.nn.gelu(x, approximate=True)

def _silu(x):
    return jax.nn.silu(x)

def _sigmoid(x):
    return jax.nn.sigmoid(x)

def _layernorm(x, axis=-1, eps=1e-05):
    m = jnp.mean(x, axis=axis, keepdims=True)
    v = jnp.var(x, axis=axis, keepdims=True)
    return (x - m) / jnp.sqrt(v + eps)

def _scatter_add(tgt, idx, src, axis=0):
    return tgt.at[idx].add(src)

def _segment_sum(src, seg, n):
    return jax.ops.segment_sum(src, seg, n)
kernel_name = 'mk_macaron_d1_jaxref_r4_9ab67a'

def setup_inputs(seed: int=0):
    np.random.seed(seed)
    _w = jnp.asarray

    def _L0_attn_setup():
        import jax, jax.numpy as jnp
        import numpy as np
        D_MODEL = 256
        D_STATE = 16
        D_CONV = 4
        EXPAND = 2
        D_INNER = EXPAND * D_MODEL
        DT_MIN, DT_MAX = (0.001, 0.1)
        BATCH, SEQ = (4, 512)

        def _silu(v):
            return v * jax.nn.sigmoid(v)
        key = jax.random.key(seed)
        ks = jax.random.split(key, 5)
        x = jax.random.normal(ks[0], (BATCH, SEQ, D_MODEL), jnp.float32)
        W_in = jax.random.normal(ks[1], (2 * D_INNER, D_MODEL), jnp.float32) / np.sqrt(D_MODEL)
        conv_w = jax.random.normal(ks[2], (D_INNER, D_CONV), jnp.float32) / np.sqrt(D_CONV)
        conv_b = jnp.zeros((D_INNER,), jnp.float32)
        W_xproj = jax.random.normal(ks[3], (2 * D_STATE + 1, D_INNER), jnp.float32) / np.sqrt(D_INNER)
        A_log = jnp.log(jnp.arange(1, D_STATE + 1, dtype=jnp.float32))
        D_param = jnp.ones((D_INNER,), jnp.float32)
        W_out = jax.random.normal(ks[4], (D_MODEL, D_INNER), jnp.float32) / np.sqrt(D_INNER)
        return dict(x=x, W_in=W_in, conv_w=conv_w, conv_b=conv_b, W_xproj=W_xproj, A_log=A_log, D_param=D_param, W_out=W_out)
    _L0_attn_in = _L0_attn_setup()

    def _L0_ffn_setup():
        import jax, jax.numpy as jnp
        import numpy as np
        NUM_EXPERTS = 8
        TOP_K = 2
        N_EMBD = 256
        B, T = (4, 512)
        key = jax.random.key(seed)
        k_x, k_g, k_e = jax.random.split(key, 3)
        x = jax.random.normal(k_x, (B, T, N_EMBD), dtype=jnp.float32)
        scale = 1.0 / np.sqrt(N_EMBD)
        gate_w = jax.random.uniform(k_g, (NUM_EXPERTS, N_EMBD), dtype=jnp.float32, minval=-scale, maxval=scale)
        expert_w = jax.random.uniform(k_e, (NUM_EXPERTS, N_EMBD, N_EMBD), dtype=jnp.float32, minval=-scale, maxval=scale)
        return {'x': x, 'gate_w': gate_w, 'expert_w': expert_w}
    _L0_ffn_in = _L0_ffn_setup()
    _d = {'L0_attn_x': _L0_attn_in['x'], 'L0_attn_W_in': _L0_attn_in['W_in'], 'L0_attn_conv_w': _L0_attn_in['conv_w'], 'L0_attn_conv_b': _L0_attn_in['conv_b'], 'L0_attn_W_xproj': _L0_attn_in['W_xproj'], 'L0_attn_A_log': _L0_attn_in['A_log'], 'L0_attn_D_param': _L0_attn_in['D_param'], 'L0_attn_W_out': _L0_attn_in['W_out'], 'L0_ffn_gate_w': _L0_ffn_in['gate_w'], 'L0_ffn_expert_w': _L0_ffn_in['expert_w']}
    _x0 = _d['L0_attn_x']
    _d['L0_attn_x'] = jax.random.normal(jax.random.fold_in(jax.random.key(seed), 1), (16, 512, 256), dtype=_x0.dtype)
    del _x0
    return _d

def reference(L0_attn_x, L0_attn_W_in, L0_attn_conv_w, L0_attn_conv_b, L0_attn_W_xproj, L0_attn_A_log, L0_attn_D_param, L0_attn_W_out, L0_ffn_gate_w, L0_ffn_expert_w):

    def _L0_attn_ref(x, W_in, conv_w, conv_b, W_xproj, A_log, D_param, W_out):
        import jax, jax.numpy as jnp
        import numpy as np
        D_MODEL = 256
        D_STATE = 16
        D_CONV = 4
        EXPAND = 2
        D_INNER = EXPAND * D_MODEL
        DT_MIN, DT_MAX = (0.001, 0.1)
        BATCH, SEQ = (4, 512)

        def _silu(v):
            return v * jax.nn.sigmoid(v)
        b, l, d = x.shape
        xz = x @ W_in.T
        x_proj, z = jnp.split(xz, 2, axis=-1)
        xp = jnp.pad(x_proj, ((0, 0), (D_CONV - 1, 0), (0, 0)))
        x_conv = conv_b + sum((xp[:, k:k + l, :] * conv_w[:, k] for k in range(D_CONV)))
        x_conv = _silu(x_conv)
        x_dbl = x_conv @ W_xproj.T
        Bmat = x_dbl[..., :D_STATE]
        Cmat = x_dbl[..., D_STATE:2 * D_STATE]
        dt = jnp.clip(jax.nn.softplus(x_dbl[..., -1]), DT_MIN, DT_MAX)
        A = -jnp.exp(A_log)

        def step(h, inp):
            x_t, dt_t, B_t, C_t = inp
            dt_A = jnp.clip(dt_t[:, None] * A, -20.0, 0.0)
            A_bar = jnp.exp(dt_A)[:, None, :]
            B_bar = jnp.clip(dt_t[:, None] * B_t, -10.0, 10.0)[:, None, :]
            h = jnp.clip(A_bar * h + B_bar * x_t[:, :, None], -100.0, 100.0)
            y_t = jnp.einsum('bds,bs->bd', h, C_t)
            return (h, y_t)
        h0 = jnp.zeros((b, D_INNER, D_STATE), x.dtype)
        xs = (jnp.swapaxes(x_conv, 0, 1), jnp.swapaxes(dt, 0, 1), jnp.swapaxes(Bmat, 0, 1), jnp.swapaxes(Cmat, 0, 1))
        _, ys = jax.lax.scan(step, h0, xs)
        y = jnp.swapaxes(ys, 0, 1)
        y = y * _silu(z) + x_conv * D_param
        return y @ W_out.T

    def _L0_ffn_ref(x, gate_w, expert_w):
        import jax, jax.numpy as jnp
        import numpy as np
        NUM_EXPERTS = 8
        TOP_K = 2
        N_EMBD = 256
        B, T = (4, 512)
        Bb, Tt, C = x.shape
        xf = x.reshape(Bb * Tt, C)
        logits = xf @ gate_w.T
        w, sel = jax.lax.top_k(logits, TOP_K)
        w = jax.nn.softmax(w.astype(jnp.float32), axis=1).astype(xf.dtype)
        n = xf.shape[0]
        w_full = jnp.zeros((n, NUM_EXPERTS), dtype=xf.dtype)
        w_full = w_full.at[jnp.arange(n)[:, None], sel].add(w)
        expert_out = jnp.einsum('nc,edc->ned', xf, expert_w)
        out = jnp.einsum('ne,ned->nd', w_full, expert_out)
        return out.reshape(Bb, Tt, C)
    x = L0_attn_x
    x = x + 0.5 * _L0_ffn_ref(_layernorm(x, axis=-1), L0_ffn_gate_w, L0_ffn_expert_w)
    x = x + _L0_attn_ref(_layernorm(x, axis=-1), L0_attn_W_in, L0_attn_conv_w, L0_attn_conv_b, L0_attn_W_xproj, L0_attn_A_log, L0_attn_D_param, L0_attn_W_out)
    x = x + 0.5 * _L0_ffn_ref(_layernorm(x, axis=-1), L0_ffn_gate_w, L0_ffn_expert_w)
    return x

_drawn_inputs = setup_inputs


def setup_inputs(seed=0):
    import zlib

    import numpy as np

    out = dict(_drawn_inputs(seed))
    spreads = {'L0_attn_conv_b': (0.0, 0.1), 'L0_attn_D_param': (1.0, 0.2)}
    factors = {}
    for name, (base, spread) in spreads.items():
        noise = np.random.default_rng([zlib.crc32(name.encode()), seed]).standard_normal(out[name].shape)
        drawn = base * np.exp(spread * noise) if base else spread * noise
        out[name] = jnp.asarray(drawn.astype(out[name].dtype))
    for name, factor in factors.items():
        out[name] = (out[name] * factor).astype(out[name].dtype)
    return out
```

```python
from contextlib import ExitStack

import numpy as np
import concourse.bass as bass
from concourse import mybir

F32 = mybir.dt.float32
F32R = mybir.dt.float32r
I32 = mybir.dt.int32
ALU = mybir.AluOpType
ACT = mybir.ActivationFunctionType
AX = mybir.AxisListType.X

P = 128
NB, T, D = 16, 512, 256
NT = T // P
KC = D // P
DI = 2 * D
NC = DI // P
NE = 8
S = 16
W = 32
NW = P // W
R8 = P // S
XD = 2 * S + 1
EPS = 1e-5
HALF_DT_MIN, HALF_DT_MAX = 0.0005, 0.05
H_LIMIT2 = 200.0
H_SAFE2 = 198.0
RANGE_SAFE = 60.0


class Signal:

    def __init__(self, sem, per):
        self.sem, self.per = sem, per

    def after(self, b, k):
        return b * self.per + (k + 1)

    def before(self, b):
        return b * self.per


def follows(b, n=1):
    return not isinstance(b, int) or b >= n


def constants():
    p = np.arange(P)
    win = p // W
    ident = np.eye(P, dtype=np.float32)
    tri = (p[:, None] <= p[None, :]).astype(np.float32)
    tail = ((p[None, :] < p[:, None]) & (win[None, :] == win[:, None])).astype(np.float32)
    member = (win[:, None] == np.arange(NW)[None, :]).astype(np.float32)
    umask = np.zeros((P, NT, R8), np.float32)
    for j in range(NT):
        umask[p, j, NW * (j % 2) + win] = 1.0
    ends = np.zeros((P, 2, NT, NT, NW), np.float32)
    for h in range(2):
        for u in range(R8):
            j, v = divmod(R8 * h + u, NW)
            rows = slice(u * S, (u + 1) * S)
            for i in range(j, NT):
                ends[rows, h, i, j, v] -= 1.0
                if i > j:
                    ends[rows, h, i, j:i, NW - 1] += 1.0
    first = np.ones((P, NT, NE), np.float32)
    first[:, :, 0] = 0.0
    parts = [ident, tri, tail, member, umask, ends, first]
    return np.concatenate([a.reshape(P, -1) for a in parts], axis=1)


CONST_COLS = [("ident", P), ("tri", P), ("tail", P), ("member", NW), ("umask", NT * R8),
              ("ends", 2 * NT * NT * NW), ("first", NT * NE)]
NCONST = sum(n for _, n in CONST_COLS)


def build(nc, x_in, w_exp, w_gate, w_in, w_xd, w_out, conv_w, conv_b, d_par, a_log, consts, out):
    F32V = lambda ap: ap.bitcast(F32)
    ctx = ExitStack()
    with ctx:
        def sb(name, shape, dt=F32):
            return ctx.enter_context(nc.sbuf_tensor(name, shape, dt))

        def signal(name, per):
            return Signal(ctx.enter_context(nc.semaphore(name)), per)

        bank = [ctx.enter_context(nc.psum_tensor(f"bank{i}", [P, 512], F32)) for i in range(8)]
        FB = [(bank[0], bank[1]), (bank[2], bank[3])]
        M1B = (bank[4], bank[5])
        M2B = (bank[6], bank[7])

        we_hi = sb("we_hi", [P, KC, NE * D], F32R)
        we_lo = sb("we_lo", [P, KC, NE * D], F32R)
        wi_hi = sb("wi_hi", [P, KC, 2 * DI], F32R)
        wi_lo = sb("wi_lo", [P, KC, 2 * DI], F32R)
        wg_hi = sb("wg_hi", [P, KC, NE], F32R)
        wg_lo = sb("wg_lo", [P, KC, NE], F32R)
        wx = sb("wx", [P, NC, XD])
        wo = sb("wo", [P, NC, D])
        wg_f = sb("wg_f", [P, KC, NE])
        cw = sb("cw", [P, NC, 4])
        cb = sb("cb", [P, NC])
        d2 = sb("d2", [P, NC])
        a2rep = sb("a2rep", [P, R8, S])
        con = sb("con", [P, NCONST])
        at, cv = 0, {}
        for name, n in CONST_COLS:
            cv[name] = con[:, at:at + n]
            at += n
        ident, tri, tail, member = cv["ident"], cv["tri"], cv["tail"], cv["member"]
        umask = cv["umask"].rearrange("p (j u) -> p j u", j=NT)
        ends = cv["ends"].rearrange("p (a e) -> p a e", a=2 * NT)
        first = cv["first"]

        xi = sb("xi", [P, NT, D])
        x1 = [sb(f"x1_{i}", [P, NT, D]) for i in range(2)]
        x1m = sb("x1m", [P, NT, D])
        x2 = sb("x2", [P, NT, D])
        x3 = sb("x3", [P, NT, D])
        stat = [sb(f"stat{l}", [P, NT, 6]) for l in range(3)]
        mv = [sb(f"mv{l}", [P, NT, 2]) for l in range(3)]
        rs = [sb(f"rs{l}", [P, 2, NT]) for l in range(3)]
        xn = [sb(f"xn{l}", [P, NT, D]) for l in range(3)]
        xT_hi = [sb(f"xT_hi{l}", [P, KC, T], F32R) for l in range(3)]
        xT_lo = [sb(f"xT_lo{l}", [P, KC, T], F32R) for l in range(3)]
        mhalf = sb("mhalf", [P, NT])
        lgT = [sb(f"lgT{f}", [NE, T]) for f in range(2)]
        lgt = [sb(f"lgt{f}", [P, NT, NE]) for f in range(2)]
        top8 = [sb(f"top8{f}", [P, NT, 8]) for f in range(2)]
        rt = [sb(f"rt{f}", [P, 8, NT, NE]) for f in range(2)]
        rt1 = [sb(f"rt1{f}", [P, 3, NT]) for f in range(2)]
        wf = [sb(f"wf{f}", [P, NT, NE]) for f in range(2)]
        etmp = [sb(f"etmp{f}", [P, 2, 2, D]) for f in range(2)]
        esum = [sb(f"esum{f}", [P, D]) for f in range(2)]

        vpre = sb("vpre", [P, 2, T])
        th = sb("th", [P, T])
        xc = [sb(f"xc{i}", [P, NC, T]) for i in range(2)]
        sz = sb("sz", [P, NC, T])
        xd = sb("xd", [XD, T])
        xmax = sb("xmax", [P, 2, NC])
        td = sb("td", [P, NT, XD])
        dts = sb("dts", [P, 8, NT])
        dta = sb("dta", [P, NT, R8, S])
        crep = sb("crep", [P, NT, R8, S])
        abc = sb("abc", [P, NT, 3, S])
        bsm = sb("bsm", [P, 3, NT, S])
        bexp = sb("bexp", [P, NT, R8, S])
        bT = sb("bT", [P, NT, P])
        lend = sb("lend", [P, NT, NW])
        lbt = sb("lbt", [P, 2 * NT, NT * NW])
        lbias = sb("lbias", [P, 2 * NT])
        ex = sb("ex", [P, T + T // 2])
        cf = sb("cf", [P, T + T // 2])
        mt = [sb(f"mt{j}", [P, T - P * j]) for j in range(NT)]
        xt = sb("xt", [P, 2, NT, P])
        t1 = sb("t1", [P, 2, T])
        yy = sb("yy", [P, NC, T])
        gsum = sb("gsum", [S, 4, NT * NW])
        bound = sb("bound", [P, 3])
        brow = sb("brow", [1, 4])
        bok = sb("bok", [1, 3])
        oki = sb("oki", [1, 1], I32)
        hst = sb("hst", [P, 3, NC, S])
        bcast = sb("bcast", [P, 8, 3, S])

        EXO = (0, T)

        scratch = nc.dram_tensor("abc_scratch", [T, 3 * S], F32)

        s_const = ctx.enter_context(nc.semaphore("s_const"))
        s_stage = [ctx.enter_context(nc.semaphore(f"s_stage{i}")) for i in range(2)]
        s_hi = ctx.enter_context(nc.semaphore("s_w_hi"))
        s_lo = ctx.enter_context(nc.semaphore("s_w_lo"))
        s_prep = ctx.enter_context(nc.semaphore("s_prep"))
        s_aexp = ctx.enter_context(nc.semaphore("s_aexp"))
        s_pconst = ctx.enter_context(nc.semaphore("s_pconst"))
        x_loaded = [signal(f"x_loaded{i}", 16) for i in range(NT)]
        x_stored = [signal(f"x_stored{i}", 16) for i in range(NT)]
        x1_kept = [signal(f"x1_kept{o}", 16) for o in range(2)]
        ln_stat = [signal(f"ln_stat{l}", 2 * NT) for l in range(3)]
        ln_rstd = [signal(f"ln_rstd{l}", 2) for l in range(3)]
        ln_xn = [signal(f"ln_xn{l}", NT) for l in range(3)]
        ln_tr = [signal(f"ln_tr{l}", KC) for l in range(3)]
        ln_hi = [signal(f"ln_hi{l}", KC) for l in range(3)]
        ln_lo = [signal(f"ln_lo{l}", KC) for l in range(3)]
        lg_mm = [signal(f"lg_mm{f}", 1) for f in range(2)]
        lg_sb = [signal(f"lg_sb{f}", 1) for f in range(2)]
        lg_tr = [signal(f"lg_tr{f}", 1) for f in range(2)]
        route = [signal(f"route{f}", 17) for f in range(2)]
        lg_exp = [signal(f"lg_exp{f}", 1) for f in range(2)]
        e_mm = [signal(f"e_mm{f}", 16) for f in range(2)]
        e_dve = [signal(f"e_dve{f}", 16) for f in range(2)]
        e_act = [signal(f"e_act{f}", 16) for f in range(2)]
        e_pool = [signal(f"e_pool{f}", 16) for f in range(2)]
        p_mm = signal("p_mm", 2 * NC)
        conv0 = signal("conv0", NC)
        conv = signal("conv", 3 * NC)
        tanh_s = signal("tanh_s", 2 * NC)
        xc_s = signal("xc_s", NC)
        xmax_s = signal("xmax_s", NC)
        sz_s = signal("sz_s", NC)
        xd_mm = signal("xd_mm", 1)
        xd_sb = signal("xd_sb", 1)
        td_tr = signal("td_tr", 1)
        td_s = signal("td_s", 1)
        dt_exp = signal("dt_exp", 1)
        dt_s = signal("dt_s", 8)
        dta_s = signal("dta_s", 2)
        bb_s = signal("bb_s", 3)
        crep_s = signal("crep_s", 1)
        eb_mm = signal("eb_mm", 1)
        eb_act = signal("eb_act", 4)
        a_exp = signal("a_exp", 1)
        bt_s = signal("bt_s", 2)
        l_mm = signal("l_mm", 1)
        lend_s = signal("lend_s", 7)
        lex_s = signal("lex_s", 4)
        c_tr = signal("c_tr", 1)
        cf_s = signal("cf_s", 2)
        bT_tr = signal("bT_tr", 1)
        bT_s = signal("bT_s", 1)
        m_mm = signal("m_mm", NT)
        m_act = signal("m_act", NT)
        m_tri = signal("m_tri", NT)
        bound_s = signal("bound_s", 7)
        bound_tr = signal("bound_tr", 1)
        ok_s = signal("ok_s", 4)
        xt_tr = signal("xt_tr", NC)
        xt_s = signal("xt_s", NC)
        y_mm = signal("y_mm", NC)
        t1_s = signal("t1_s", NC)
        y_checked = signal("y_checked", NC)
        yy_s = signal("yy_s", NC)
        o_mm = signal("o_mm", 2)
        x2_s = signal("x2_s", 2)
        slow = ctx.enter_context(nc.semaphore("slow_step"))
        slow_dma = ctx.enter_context(nc.semaphore("slow_dma"))

        def apart(eng):
            eng.nop(nofuse=True)

        block = ctx.enter_context(nc.Block())

        HALF_E = NE * D // 2
        def pieces():
            return [
                (w_exp[:, :, 0:HALF_E], we_hi[:, :, 0:HALF_E], we_lo[:, :, 0:HALF_E]),
                (w_exp[:, :, HALF_E:2 * HALF_E], we_hi[:, :, HALF_E:2 * HALF_E], we_lo[:, :, HALF_E:2 * HALF_E]),
                (w_in, wi_hi[:, :, :], wi_lo[:, :, :]),
            ]
        staging = [xc[i][:, :, :].rearrange("p a b -> p (a b)").rearrange("p (k n) -> p k n", k=KC) for i in range(2)]
        NSMALL = 8

        def x_of(l, b_par):
            return (xi, x1[b_par], x2)[l]


        LAGS = {"R1": 1, "F1": 0, "M1": -1, "M2": -2, "F2": -3}
        SLOTS = 20
        F1_STEPS = {slot: (4 + slot,) for slot in range(16)}
        R1_STEPS = {16: (0, 1), 17: (2,), 18: (3,)}
        F2_STEPS = {0: (0,), 1: (1,), 2: (2,), 3: (3,), 5: (4,), 6: (5,), 7: (6,), 8: (7, 8), 9: (9,), 10: (10,),
                    11: (11,), 12: (12, 13), 13: (14,), 14: (15,), 15: (16,), 16: (17,), 17: (18,), 19: (19,)}
        LN_STAT = ((6, 10, 12, 14), (6, 10, 14, 18), (17, 17, 17, 17))
        LN_APPLY = (15, 2, 18)
        TURN_SLOTS, X_SLOTS, XD_SLOT, TOK_SLOT, DT_SLOT, Z_SLOTS = (3, 4), (5, 7, 9, 11), 13, 15, 16, (14, 16, 17, 18)
        END_SLOT, SUM_SLOT, C_SLOT, CF_SLOT, BT_SLOT, M_SLOTS = 0, 1, 2, 3, 4, (5, 6, 7, 8)
        BOUND_SLOT, XT_SLOTS, Y_SLOTS, O_SLOTS = 9, (9, 10, 12, 13), (10, 11, 13, 14), (15, 16)
        LOOP0, LOOP1 = 4, 14

        def run(eng, emit):
            def on(it):
                return {n for n, lag in LAGS.items() if 0 <= it + lag < NB}
            for it in range(-1, LOOP0):
                emit(it, it % 2, on(it))
            with eng.Fori(0, (LOOP1 - LOOP0) // 2) as pair:
                emit(pair * 2 + LOOP0, LOOP0 % 2, set(LAGS))
                emit(pair * 2 + (LOOP0 + 1), (LOOP0 + 1) % 2, set(LAGS))
            for it in range(LOOP1, NB + 3):
                emit(it, it % 2, on(it))

        @block.sync
        def _(sp):
            small = [(con[:, :], consts), (wg_f[:, :, :], w_gate), (wx[:, :, :], w_xd), (wo[:, :, :], w_out),
                     (cw[:, :, :], conv_w), (cb[:, :], conv_b), (d2[:, :], d_par),
                     (a2rep[:, 0, :], a_log)]
            assert len(small) == NSMALL
            for n, (src, hi, lo) in enumerate(pieces()):
                if n >= 2:
                    sp.wait_ge(s_lo, n - 1)
                sp.dma_start(staging[n % 2], src).then_inc(s_stage[n % 2], 16)
                if n == 1:
                    for dst, src in small:
                        sp.dma_start(dst, src).then_inc(s_const, 16)

            def load(b, i):
                if follows(b):
                    sp.wait_ge(e_dve[0].sem, e_dve[0].after(b - 1, 4 * i))
                    apart(sp)
                    sp.wait_ge(ln_xn[0].sem, ln_xn[0].after(b - 1, i))
                    apart(sp)
                    if follows(b):
                        sp.wait_ge(x_loaded[i].sem, x_loaded[i].before(b))
                    apart(sp)
                sp.dma_start(xi[:, i, :], x_in[bass.ds(b * T + i * P, P), :]).then_inc(x_loaded[i].sem, 16)

            def store(b, i):
                sp.wait_ge(e_pool[1].sem, e_pool[1].after(b, 4 * i + 3))
                apart(sp)
                if follows(b):
                    sp.wait_ge(x_stored[i].sem, x_stored[i].before(b))
                    apart(sp)
                sp.dma_start(out[bass.ds(b * T + i * P, P), :], x3[:, i, :]).then_inc(x_stored[i].sem, 16)

            def keep(b, par, o):
                sp.wait_ge(e_pool[0].sem, e_pool[0].after(b, 8 * o + 7))
                apart(sp)
                if follows(b):
                    sp.wait_ge(x2_s.sem, x2_s.after(b - 1, o))
                    apart(sp)
                    sp.wait_ge(x1_kept[o].sem, x1_kept[o].before(b))
                    apart(sp)
                two = slice(2 * o, 2 * o + 2)
                sp.dma_start(x1m[:, two, :], x1[par][:, two, :]).then_inc(x1_kept[o].sem, 16)

            def emit(it, par, on):
                for what in ("load", 0), ("load", 1), ("load", 2), ("store", 0), ("load", 3), ("store", 1), ("keep", 0), \
                        ("store", 2), ("keep", 1), ("store", 3):
                    if what[0] == "load" and "R1" in on:
                        load(it + 1, what[1])
                    elif what[0] == "store" and "F2" in on:
                        store(it - 3, what[1])
                    elif what[0] == "keep" and "M1" in on:
                        keep(it - 1, (par + 1) % 2, what[1])
            run(sp, emit)
            for i in range(NT):
                sp.wait_ge(x_stored[i].sem, NB * 16)

        @block.tensor
        def _(pe):
            def three(dst, a_hi, a_lo, b_hi, b_lo, k, n):
                pe.matmul(dst, a_hi, b_lo, start=(k == 0), stop=False)
                pe.matmul(dst, a_lo, b_hi, start=False, stop=False)
                return pe.matmul(dst, a_hi, b_hi, start=False, stop=(k == n - 1))

            def ln_transpose(l, b, c, dst):
                pe.wait_ge(ln_xn[l].sem, ln_xn[l].after(b, NT - 1))
                for i in range(NT):
                    mm = pe.transpose(dst[:, i * P:(i + 1) * P], xn[l][:, i, c * P:(c + 1) * P], ident)
                mm.then_inc(ln_tr[l].sem, 1)

            def moe(f, b, slot):
                l = 2 * f
                A, B = FB[f]
                if slot == 0:
                    if follows(b):
                        pe.wait_ge(e_dve[f].sem, e_dve[f].before(b))
                    ln_transpose(l, b, 0, A)
                elif slot == 1:
                    if follows(b):
                        pe.wait_ge(e_act[f].sem, e_act[f].before(b))
                    ln_transpose(l, b, 1, B)
                elif slot == 2:
                    pe.wait_ge(ln_lo[l].sem, ln_lo[l].after(b, 1))
                    for c in range(KC):
                        mm = three(A[0:NE, :], wg_hi[:, c, :], wg_lo[:, c, :],
                                   xT_hi[l][:, c, :], xT_lo[l][:, c, :], c, KC)
                    mm.then_inc(lg_mm[f].sem, 1)
                elif slot == 3:
                    pe.wait_ge(lg_sb[f].sem, lg_sb[f].after(b, 0))
                    apart(pe)
                    for i in range(NT):
                        mm = pe.transpose(B[:, i * NE:(i + 1) * NE], lgT[f][:, i * P:(i + 1) * P], ident[0:NE, 0:NE])
                    mm.then_inc(lg_tr[f].sem, 1)
                else:
                    g = slot - 4
                    i, p = divmod(g, 4)
                    dst = (A, B)[p % 2]
                    if g == 0:
                        pe.wait_ge(lg_sb[f].sem, lg_sb[f].after(b, 0))
                    elif g == 1:
                        pe.wait_ge(route[f].sem, route[f].after(b, 0))
                    elif g % 2 == 0:
                        pe.wait_ge(e_dve[f].sem, e_dve[f].after(b, g - 1))
                    else:
                        pe.wait_ge(e_act[f].sem, e_act[f].after(b, g - 2))
                    for c in range(KC):
                        cols = slice(p * 2 * D, (p + 1) * 2 * D)
                        mm = three(dst[:, :], xT_hi[l][:, c, i * P:(i + 1) * P], xT_lo[l][:, c, i * P:(i + 1) * P],
                                   we_hi[:, c, cols], we_lo[:, c, cols], c, KC)
                    mm.then_inc(e_mm[f].sem, 1)

            def project(b, n, dst):
                for c in range(KC):
                    cols = slice(n * P, (n + 1) * P)
                    mm = three(dst[:, :], wi_hi[:, c, cols], wi_lo[:, c, cols],
                               xT_hi[1][:, c, :], xT_lo[1][:, c, :], c, KC)
                mm.then_inc(p_mm.sem, 1)

            def m1(b, par, slot):
                A, B = M1B
                X = xc[par]
                if slot == TURN_SLOTS[0]:
                    if follows(b):
                        pe.wait_ge(sz_s.sem, sz_s.before(b))
                    ln_transpose(1, b, 0, A)
                elif slot == TURN_SLOTS[1]:
                    ln_transpose(1, b, 1, B)
                elif slot in X_SLOTS:
                    n = X_SLOTS.index(slot)
                    if n == 0:
                        pe.wait_ge(ln_lo[1].sem, ln_lo[1].after(b, 1))
                    dst = (A, B)[n % 2]
                    if n >= 2:
                        pe.wait_ge(conv.sem, conv.after(b, 3 * (n - 2) + 2))
                    project(b, n, dst)
                elif slot == XD_SLOT:
                    pe.wait_ge(conv.sem, conv.after(b, 3 * 2 + 2))
                    for c in range(NC):
                        pe.wait_ge(xc_s.sem, xc_s.after(b, c))
                        mm = pe.matmul(A[0:XD, :], wx[:, c, :], X[:, c, :], start=(c == 0), stop=(c == NC - 1))
                    mm.then_inc(xd_mm.sem, 1)
                elif slot == TOK_SLOT:
                    pe.wait_ge(xd_sb.sem, xd_sb.after(b, 0))
                    apart(pe)
                    for j in range(NT):
                        mm = pe.transpose(A[:, j * XD:(j + 1) * XD], xd[:, j * P:(j + 1) * P], ident[0:XD, 0:XD])
                    mm.then_inc(td_tr.sem, 1)
                elif slot in Z_SLOTS:
                    n = Z_SLOTS.index(slot)
                    dst = (B, A)[n % 2]
                    if n == 0:
                        pe.wait_ge(conv.sem, conv.after(b, 3 * 3 + 2))
                    elif n == 1:
                        pe.wait_ge(td_s.sem, td_s.after(b, 0))
                    else:
                        pe.wait_ge(sz_s.sem, sz_s.after(b, n - 2))
                    project(b, NC + n, dst)

            def m2(b, par, slot):
                A, B = M2B
                X = xc[par]
                if slot == END_SLOT:
                    if follows(b):
                        pe.wait_ge(x2_s.sem, x2_s.before(b))
                    pe.wait_ge(dta_s.sem, dta_s.after(b, 1))
                    pe.matmul(B[:, 0:NT * S], tail, dta[:, :, 0, :], start=True, stop=True)
                    pe.wait_ge(bb_s.sem, bb_s.after(b, 2))
                    for j in range(NT):
                        pe.matmul(B[0:S, 64 + NW * j:64 + NW * (j + 1)], bsm[:, 0, j, :], member, start=True, stop=True)
                        mm = pe.matmul(B[0:S, 80 + NW * j:80 + NW * (j + 1)], dta[:, j, 0, :], member,
                                       start=True, stop=True)
                    mm.then_inc(eb_mm.sem, 1)
                elif slot == SUM_SLOT:
                    for j in range(NT):
                        mm = pe.matmul(A[:, j * P:(j + 1) * P], dta[:, j, :, :].rearrange("p u s -> p (u s)"), tri,
                                       start=True, stop=True)
                    mm.then_inc(l_mm.sem, 1)
                elif slot == C_SLOT:
                    pe.wait_ge(eb_act.sem, eb_act.after(b, 3))
                    pe.wait_ge(crep_s.sem, crep_s.after(b, 0))
                    for j in range(NT):
                        mm = pe.transpose(B[:, j * P:(j + 1) * P], crep[:, j, :, :].rearrange("p u s -> p (u s)"), ident)
                    mm.then_inc(c_tr.sem, 1)
                elif slot == BT_SLOT:
                    pe.wait_ge(lex_s.sem, lex_s.after(b, 3))
                    pe.wait_ge(bt_s.sem, bt_s.after(b, 1))
                    for j in range(NT):
                        mm = pe.transpose(A[:, j * P:(j + 1) * P], bexp[:, j, :, :].rearrange("p u s -> p (u s)"), ident)
                    mm.then_inc(bT_tr.sem, 1)
                elif slot in M_SLOTS:
                    j = M_SLOTS.index(slot)
                    dst = (B, A)[j % 2]
                    if j == 0:
                        pe.wait_ge(cf_s.sem, cf_s.after(b, 1))
                        pe.wait_ge(bT_s.sem, bT_s.after(b, 0))
                    elif j >= 2:
                        pe.wait_ge(m_act.sem, m_act.after(b, j - 2))
                    h = j // 2
                    lo = EXO[h] + P * j - 2 * P * h
                    n = T - P * j
                    pe.matmul(dst[:, 0:n], bT[:, j, :], cf[:, lo:lo + n], start=True, stop=True)\
                      .then_inc(m_mm.sem, 1)
                if slot == BOUND_SLOT:
                    pe.wait_ge(m_act.sem, m_act.after(b, 2))
                    pe.wait_ge(bound_s.sem, bound_s.after(b, 6))
                    for k in range(3):
                        mm = pe.transpose(B[0:1, k * P:(k + 1) * P], bound[:, k:k + 1], ident)
                    mm.then_inc(bound_tr.sem, 1)
                if slot in XT_SLOTS:
                    c = XT_SLOTS.index(slot)
                    if c == 0:
                        pe.wait_ge(m_act.sem, m_act.after(b, 3))
                        dst = A
                    elif c == 1:
                        pe.wait_ge(ok_s.sem, ok_s.after(b, 0))
                        dst = B
                    else:
                        dst = (A, B)[c % 2]
                        pe.wait_ge(t1_s.sem, t1_s.after(b, c - 2))
                    pe.wait_ge(xc_s.sem, xc_s.after(b, c))
                    for j in range(NT):
                        mm = pe.transpose(dst[:, j * P:(j + 1) * P], X[:, c, j * P:(j + 1) * P], ident)
                    mm.then_inc(xt_tr.sem, 1)
                if slot in Y_SLOTS:
                    c = Y_SLOTS.index(slot)
                    dst = (A, B)[c % 2]
                    pe.wait_ge(xt_s.sem, xt_s.after(b, c))
                    if c == 0:
                        pe.wait_ge(m_tri.sem, m_tri.after(b, NT - 1))
                    for j in range(NT):
                        mm = pe.matmul(dst[:, P * j:T], xt[:, c % 2, j, :], mt[j][:, :],
                                       start=(j == 0), stop=(j == NT - 1), skip_group_check=True)
                    mm.then_inc(y_mm.sem, 1)
                if slot in O_SLOTS:
                    o = O_SLOTS.index(slot)
                    dst = (A, B)[o]
                    pe.wait_ge(t1_s.sem, t1_s.after(b, 2 + o))
                    pe.wait_ge(yy_s.sem, yy_s.after(b, NC - 1))
                    for q in range(2):
                        i = 2 * o + q
                        for c in range(NC):
                            mm = pe.matmul(dst[:, q * D:(q + 1) * D], yy[:, c, i * P:(i + 1) * P], wo[:, c, :],
                                           start=(c == 0), stop=(c == NC - 1))
                    mm.then_inc(o_mm.sem, 1)

            pe.wait_ge(s_const, 16 * NSMALL)
            pe.wait_ge(s_lo, len(pieces()) + 1)
            pe.wait_ge(s_prep, 5)

            def emit(it, par, on):
                for slot in range(SLOTS):
                    for step in F1_STEPS.get(slot, ()) if "F1" in on else ():
                        moe(0, it, step)
                    for step in R1_STEPS.get(slot, ()) if "R1" in on else ():
                        moe(0, it + 1, step)
                    if "M2" in on:
                        m2(it - 2, par, slot)
                    for step in F2_STEPS.get(slot, ()) if "F2" in on else ():
                        moe(1, it - 3, step)
                    if "M1" in on:
                        m1(it - 1, (par + 1) % 2, slot)
            run(pe, emit)

        @block.scalar
        def _(act):
            for n, (src, hi, lo) in enumerate(pieces()):
                act.wait_ge(s_stage[n % 2], 16 * (n // 2 + 1))
                act.activation(hi, staging[n % 2], ACT.Copy).then_inc(s_hi, 1)
            act.wait_ge(s_const, 16 * NSMALL)
            act.activation(wg_hi[:, :, :], wg_f[:, :, :], ACT.Copy).then_inc(s_hi, 1)
            act.activation(a2rep[:, 1, :], a2rep[:, 0, :], ACT.Exp).then_inc(s_aexp, 1)

            def ln_hi_part(l, b, c, bank_):
                if c == 0:
                    reads = p_mm if l == 1 else e_mm[l // 2]
                    if follows(b):
                        act.wait_ge(reads.sem, reads.before(b))
                act.wait_ge(ln_tr[l].sem, ln_tr[l].after(b, c))
                act.activation(xT_hi[l][:, c, :], bank_[:, :], ACT.Copy).then_inc(ln_hi[l].sem, 1)

            def moe(f, b, slot):
                A, B = FB[f]
                if slot < 2:
                    ln_hi_part(2 * f, b, slot, FB[f][slot])
                elif slot == 2:
                    if follows(b):
                        act.wait_ge(lg_tr[f].sem, lg_tr[f].before(b))
                    act.wait_ge(lg_mm[f].sem, lg_mm[f].after(b, 0))
                    act.activation(lgT[f][:, :], A[0:NE, :], ACT.Copy).then_inc(lg_sb[f].sem, 1)
                elif slot == 3:
                    act.wait_ge(route[f].sem, route[f].after(b, 5))
                    act.activation(rt[f][:, 1], rt[f][:, 0], ACT.Exp).then_inc(lg_exp[f].sem, 1)
                elif slot % 2 == 1:
                    g = slot - 4
                    i, p = divmod(g, 4)
                    o = g // 2
                    act.wait_ge(e_mm[f].sem, e_mm[f].after(b, g))
                    if g == 1:
                        act.wait_ge(route[f].sem, route[f].after(b, 16))
                    if i == 0:
                        if follows(b):
                            act.wait_ge(e_pool[f].sem, e_pool[f].before(b))
                    else:
                        act.wait_ge(e_pool[f].sem, e_pool[f].after(b, 4 * (i - 1) + (0 if p == 1 else 2)))
                    for q in range(2):
                        act.activation(etmp[f][:, o % 2, q, :], B[:, q * D:(q + 1) * D], ACT.Copy,
                                       scale=wf[f][:, i, 2 * p + q:2 * p + q + 1]).then_inc(e_act[f].sem, 1)

            def m1(b, par, slot):
                A, B = M1B
                X = xc[par]
                if slot in TURN_SLOTS:
                    c = TURN_SLOTS.index(slot)
                    ln_hi_part(1, b, c, M1B[c])
                elif slot in X_SLOTS:
                    n = X_SLOTS.index(slot)
                    src = (A, B)[n % 2]
                    act.wait_ge(p_mm.sem, p_mm.after(b, n))
                    if n < 2:
                        if follows(b):
                            act.wait_ge(xc_s.sem, xc_s.before(b))
                    else:
                        act.wait_ge(xc_s.sem, xc_s.after(b, n - 2))
                    act.activation(vpre[:, n % 2, :], src[:, :], ACT.Identity, bias=cb[:, n:n + 1],
                                   scale=cw[:, n, 3:4]).then_inc(conv0.sem, 1)
                if slot - 1 in X_SLOTS:
                    n = X_SLOTS.index(slot - 1)
                    act.wait_ge(conv.sem, conv.after(b, 3 * n + 2))
                    if n == 0:
                        if follows(b):
                            act.wait_ge(sz_s.sem, sz_s.before(b))
                    else:
                        act.wait_ge(xc_s.sem, xc_s.after(b, n - 1))
                    act.activation(th[:, :], vpre[:, n % 2, :], ACT.Tanh, scale=0.5).then_inc(tanh_s.sem, 1)
                elif slot == XD_SLOT:
                    if follows(b):
                        act.wait_ge(td_tr.sem, td_tr.before(b))
                    act.wait_ge(xd_mm.sem, xd_mm.after(b, 0))
                    act.activation(xd[:, :], A[0:XD, :], ACT.Copy).then_inc(xd_sb.sem, 1)
                elif slot == TOK_SLOT:
                    act.wait_ge(td_tr.sem, td_tr.after(b, 0))
                    if follows(b):
                        act.wait_ge(y_checked.sem, y_checked.before(b))
                    if follows(b):
                        act.wait_ge(dt_s.sem, dt_s.before(b))
                    if follows(b):
                        act.wait_ge(bb_s.sem, bb_s.before(b))
                    if follows(b):
                        act.wait_ge(crep_s.sem, crep_s.before(b))
                    act.activation(td[:, :, :], A[:, 0:NT * XD].rearrange("p (j r) -> p j r", j=NT),
                                   ACT.Copy).then_inc(td_s.sem, 1)
                    act.wait_ge(td_s.sem, td_s.after(b, 0))
                    act.activation(dts[:, 0, :], td[:, :, 2 * S], ACT.Exp).then_inc(dt_exp.sem, 1)
                elif slot in Z_SLOTS:
                    n = Z_SLOTS.index(slot)
                    src = (B, A)[n % 2]
                    act.wait_ge(p_mm.sem, p_mm.after(b, NC + n))
                    if n == 0:
                        act.wait_ge(xc_s.sem, xc_s.after(b, NC - 1))
                    else:
                        act.wait_ge(sz_s.sem, sz_s.after(b, n - 1))
                    act.activation(th[:, :], src[:, :], ACT.Tanh, scale=0.5).then_inc(tanh_s.sem, 1)

            def m2(b, par, slot):
                A, B = M2B
                if slot == END_SLOT:
                    act.wait_ge(eb_mm.sem, eb_mm.after(b, 0))
                    if follows(b):
                        act.wait_ge(bt_s.sem, bt_s.before(b))
                    act.activation(bsm[:, 1, :, :], B[:, 0:NT * S].rearrange("p (j s) -> p j s", j=NT),
                                   ACT.Exp).then_inc(eb_act.sem, 1)
                    if follows(b):
                        act.wait_ge(bound_s.sem, bound_s.before(b))
                    act.activation(gsum[:, 0, :], B[0:S, 64:80], ACT.Copy).then_inc(eb_act.sem, 1)
                    act.activation(gsum[:, 1, :], B[0:S, 80:96], ACT.Exp).then_inc(eb_act.sem, 1)
                    act.activation(gsum[:, 2, :], B[0:S, 80:96], ACT.Copy).then_inc(eb_act.sem, 1)
                elif slot == SUM_SLOT:
                    act.activation(abc[:, :, 0, :], dta[:, :, 0, :], ACT.Exp).then_inc(a_exp.sem, 1)
                elif slot == C_SLOT:
                    act.wait_ge(lend_s.sem, lend_s.after(b, 6))
                    for i in (2, 3):
                        act.activation(ex[:, i * P:(i + 1) * P], A[:, i * P:(i + 1) * P], ACT.Exp,
                                       bias=lbias[:, i:i + 1]).then_inc(lex_s.sem, 1)
                    for h in range(2):
                        own = ex[:, EXO[h]:EXO[h] + 2 * P]
                        act.activation(own, own, ACT.Exp).then_inc(lex_s.sem, 1)
                elif slot == BT_SLOT:
                    if follows(b):
                        act.wait_ge(m_mm.sem, m_mm.before(b))
                    act.wait_ge(bT_tr.sem, bT_tr.after(b, 0))
                    act.activation(bT[:, :, :], A[:, :].rearrange("p (j t) -> p j t", j=NT), ACT.Copy)\
                       .then_inc(bT_s.sem, 1)
                elif slot in M_SLOTS:
                    j = M_SLOTS.index(slot)
                    if j == 0:
                        if follows(b):
                            act.wait_ge(y_mm.sem, y_mm.before(b))
                    act.wait_ge(m_mm.sem, m_mm.after(b, j))
                    act.activation(mt[j][:, :], (B, A)[j % 2][:, 0:T - P * j], ACT.Copy).then_inc(m_act.sem, 1)
                elif slot in XT_SLOTS:
                    c = XT_SLOTS.index(slot)
                    act.wait_ge(xt_tr.sem, xt_tr.after(b, c))
                    if c < 2:
                        if follows(b):
                            act.wait_ge(y_mm.sem, y_mm.before(b))
                    else:
                        act.wait_ge(y_mm.sem, y_mm.after(b, c - 2))
                    act.activation(xt[:, c % 2, :, :], (A, B)[c % 2][:, :].rearrange("p (j t) -> p j t", j=NT),
                                   ACT.Copy).then_inc(xt_s.sem, 1)

            def emit(it, par, on):
                for slot in range(SLOTS):
                    for step in F1_STEPS.get(slot, ()) if "F1" in on else ():
                        moe(0, it, step)
                    for step in R1_STEPS.get(slot, ()) if "R1" in on else ():
                        moe(0, it + 1, step)
                    if "M2" in on:
                        m2(it - 2, par, slot)
                    for step in F2_STEPS.get(slot, ()) if "F2" in on else ():
                        moe(1, it - 3, step)
                    if "M1" in on:
                        m1(it - 1, (par + 1) % 2, slot)
            run(act, emit)

        @block.vector
        def _(dve):
            for n, (src, hi, lo) in enumerate(pieces()):
                dve.wait_ge(s_hi, n + 1)
                dve.tensor_tensor(lo, staging[n % 2], F32V(hi), ALU.subtract).then_inc(s_lo, 1)
            dve.wait_ge(s_hi, len(pieces()) + 1)
            dve.tensor_tensor(wg_lo[:, :, :], wg_f[:, :, :], F32V(wg_hi[:, :, :]), ALU.subtract).then_inc(s_lo, 1)
            dve.tensor_scalar(wx[:, :, :], wx[:, :, :], 0.5, None, ALU.mult).then_inc(s_prep, 1)
            dve.tensor_scalar(wo[:, :, :], wo[:, :, :], 0.25, None, ALU.mult).then_inc(s_prep, 1)
            dve.tensor_scalar(d2[:, :], d2[:, :], 2.0, None, ALU.mult).then_inc(s_prep, 1)
            dve.wait_ge(s_aexp, 1)
            dve.tensor_scalar(a2rep[:, 2:R8, :], a2rep[:, 1:2, :].to_broadcast([P, R8 - 2, S]), -2.0, None, ALU.mult)\
               .then_inc(s_prep, 1)
            dve.wait_ge(s_prep, 4)
            dve.tensor_copy(a2rep[:, 0:2, :], a2rep[:, 2:4, :]).then_inc(s_prep, 1)
            dve.memset(bound[:, :], 0.0).then_inc(s_prep, 1)
            dve.wait_ge(s_prep, 6)

            def ln_stats(l, b, par, i):
                if l == 0:
                    dve.wait_ge(x_loaded[i].sem, x_loaded[i].after(b, 15))
                elif l == 1:
                    dve.wait_ge(e_pool[0].sem, e_pool[0].after(b, 4 * i + 3))
                else:
                    dve.wait_ge(x2_s.sem, x2_s.after(b, i // 2))
                dve.bn_stats(stat[l][:, i, :], x_of(l, par)[:, i, :]).then_inc(ln_stat[l].sem, 1)

            def ln_moments(l, b):
                for i in range(NT):
                    dve.wait_ge(ln_stat[l].sem, ln_stat[l].after(b, i))
                    apart(dve)
                    dve.bn_aggr(mv[l][:, i, :], stat[l][:, i, :]).then_inc(ln_stat[l].sem, 1)

            def ln_apply(l, b, par):
                X = x_of(l, par)
                dve.wait_ge(ln_rstd[l].sem, ln_rstd[l].after(b, 1))
                for i in range(NT):
                    dve.tensor_scalar(xn[l][:, i, :], X[:, i, :], mv[l][:, i, 0:1], rs[l][:, 1, i:i + 1],
                                      ALU.subtract, ALU.mult).then_inc(ln_xn[l].sem, 1)

            def ln_lo_part(l, b, c, bank_):
                dve.wait_ge(ln_hi[l].sem, ln_hi[l].after(b, c))
                dve.tensor_tensor(xT_lo[l][:, c, :], bank_[:, :], F32V(xT_hi[l][:, c, :]), ALU.subtract)\
                   .then_inc(ln_lo[l].sem, 1)

            def router(f, b, B):
                r = route[f]
                L, m8, small, one = lgt[f], top8[f], rt[f], rt1[f]
                inc = lambda ins: ins.then_inc(r.sem, 1)
                bc = lambda ap: ap.to_broadcast([P, NT, NE])
                dve.wait_ge(lg_tr[f].sem, lg_tr[f].after(b, 0))
                inc(dve.tensor_copy(L[:, :, :], B[:, 0:NT * NE].rearrange("p (i e) -> p i e", i=NT)))
                dve.wait_ge(r.sem, r.after(b, 0))
                apart(dve)
                for i in range(NT):
                    inc(dve.max(m8[:, i, :], L[:, i, :]))
                dve.wait_ge(r.sem, r.after(b, 4))
                m1, m2 = bc(m8[:, :, 0:1]), bc(m8[:, :, 1:2])
                inc(dve.tensor_tensor(small[:, 0], L[:, :, :], m1, ALU.subtract))
                inc(dve.tensor_tensor(small[:, 2], L[:, :, :], m2, ALU.is_gt))
                inc(dve.tensor_tensor(small[:, 3], L[:, :, :], m2, ALU.is_equal))
                inc(dve.tensor_tensor(one[:, 0, :], m8[:, :, 0], m8[:, :, 1], ALU.is_gt))
                dve.wait_ge(r.sem, r.after(b, 7))
                inc(dve.tensor_tensor_scan(small[:, 4].rearrange("p i e -> p (i e)"), first,
                                           small[:, 3].rearrange("p i e -> p (i e)"), 0.0, ALU.mult, ALU.add))
                dve.wait_ge(r.sem, r.after(b, 9))
                inc(dve.tensor_tensor(small[:, 5], small[:, 4], bc(one[:, 0, :].unsqueeze(2)), ALU.add))
                dve.wait_ge(r.sem, r.after(b, 10))
                inc(dve.scalar_tensor_tensor(small[:, 6], small[:, 5], 2.0, small[:, 3], ALU.is_le, ALU.mult))
                dve.wait_ge(r.sem, r.after(b, 11))
                inc(dve.tensor_tensor(small[:, 7], small[:, 6], small[:, 2], ALU.add))
                dve.wait_ge(r.sem, r.after(b, 12))
                dve.wait_ge(lg_exp[f].sem, lg_exp[f].after(b, 0))
                inc(dve.tensor_tensor(small[:, 5], small[:, 7], small[:, 1], ALU.mult))
                dve.wait_ge(r.sem, r.after(b, 13))
                inc(dve.tensor_reduce(one[:, 1, :], small[:, 5], AX, ALU.add))
                dve.wait_ge(r.sem, r.after(b, 14))
                inc(dve.reciprocal(one[:, 2, :], one[:, 1, :]))
                dve.wait_ge(r.sem, r.after(b, 15))
                if follows(b):
                    dve.wait_ge(e_dve[f].sem, e_dve[f].before(b))
                if follows(b):
                    dve.wait_ge(e_act[f].sem, e_act[f].before(b))
                inc(dve.scalar_tensor_tensor(wf[f][:, :, :], small[:, 5], 0.5, bc(one[:, 2, :].unsqueeze(2)),
                                             ALU.mult, ALU.mult))
                dve.wait_ge(r.sem, r.after(b, 16))

            def moe(f, b, par, slot):
                l = 2 * f
                A, B = FB[f]
                X0 = xi if f == 0 else x2
                X = x1[par] if f == 0 else x3
                if slot < 2:
                    if slot == 0:
                        if follows(b):
                            dve.wait_ge(e_mm[f].sem, e_mm[f].before(b))
                    ln_lo_part(l, b, slot, FB[f][slot])
                elif slot == 3:
                    router(f, b, B)
                elif slot >= 4 and slot % 2 == 0:
                    g = slot - 4
                    i, p = divmod(g, 4)
                    if p == 0:
                        if f == 0:
                            if follows(b, 2):
                                dve.wait_ge(x1_kept[i // 2].sem, x1_kept[i // 2].before(b - 1))
                        elif follows(b):
                            dve.wait_ge(x_stored[i].sem, b * 16)
                    dve.wait_ge(e_mm[f].sem, e_mm[f].after(b, g))
                    for q in range(2):
                        k = g + q
                        if p + q > 0:
                            dve.wait_ge(e_dve[f].sem, e_dve[f].after(b, k - 1))
                        e = 2 * p + q
                        src = X0 if p + q == 0 else X
                        dve.scalar_tensor_tensor(X[:, i, :], A[:, q * D:(q + 1) * D], wf[f][:, i, e:e + 1],
                                                 src[:, i, :], ALU.mult, ALU.add).then_inc(e_dve[f].sem, 1)

            def m1(b, par, slot):
                A, B = M1B
                X = xc[par]
                bc_s = lambda ap: ap.unsqueeze(2).to_broadcast([P, NT, S])
                if slot == DT_SLOT:
                    inc = lambda ins: ins.then_inc(dt_s.sem, 1)
                    dve.wait_ge(dt_exp.sem, dt_exp.after(b, 0))
                    if follows(b):
                        dve.wait_ge(dta_s.sem, dta_s.before(b))
                    if follows(b):
                        dve.wait_ge(bb_s.sem, bb_s.before(b))
                    u, w, r_, r, q, p1, p2, hdt = (dts[:, k, :] for k in range(8))
                    inc(dve.tensor_scalar(w, u, 0.2, 2.0, ALU.min, ALU.add))
                    dve.wait_ge(dt_s.sem, dt_s.after(b, 0))
                    inc(dve.reciprocal(r_, w))
                    dve.wait_ge(dt_s.sem, dt_s.after(b, 1))
                    inc(dve.scalar_tensor_tensor(r, u, 0.2, r_, ALU.min, ALU.mult))
                    dve.wait_ge(dt_s.sem, dt_s.after(b, 2))
                    inc(dve.tensor_tensor(q, r, r, ALU.mult))
                    dve.wait_ge(dt_s.sem, dt_s.after(b, 3))
                    inc(dve.tensor_scalar(p1, q, 1.0 / 5, 1.0 / 3, ALU.mult, ALU.add))
                    dve.wait_ge(dt_s.sem, dt_s.after(b, 4))
                    inc(dve.tensor_tensor(p2, p1, q, ALU.mult))
                    dve.wait_ge(dt_s.sem, dt_s.after(b, 5))
                    inc(dve.scalar_tensor_tensor(p1, p2, 1.0, r, ALU.add, ALU.mult))
                    dve.wait_ge(dt_s.sem, dt_s.after(b, 6))
                    inc(dve.tensor_scalar(hdt, p1, HALF_DT_MIN, HALF_DT_MAX, ALU.max, ALU.min))
                    dve.wait_ge(dt_s.sem, dt_s.after(b, 7))
                    if follows(b):
                        dve.wait_ge(lex_s.sem, lex_s.before(b))
                    if follows(b):
                        dve.wait_ge(a_exp.sem, a_exp.before(b))
                    if follows(b):
                        dve.wait_ge(l_mm.sem, l_mm.before(b))
                    flat = lambda t: t[:, :, :, :].rearrange("p j u s -> p j (u s)")
                    dve.tensor_tensor(flat(dta), hdt.unsqueeze(2).to_broadcast([P, NT, P]),
                                      a2rep[:, :, :].rearrange("p u s -> p (u s)").unsqueeze(1).to_broadcast([P, NT, P]),
                                      ALU.mult).then_inc(dta_s.sem, 1)
                    dve.scalar_tensor_tensor(bsm[:, 2, :, :], td[:, :, 0:S], 2.0, bc_s(hdt), ALU.mult, ALU.mult)\
                       .then_inc(bb_s.sem, 1)
                    dve.wait_ge(dta_s.sem, dta_s.after(b, 0))
                    dve.tensor_scalar(flat(dta), flat(dta), -20.0, 0.0, ALU.max, ALU.min).then_inc(dta_s.sem, 1)
                    dve.wait_ge(bb_s.sem, bb_s.after(b, 0))
                    if follows(b):
                        dve.wait_ge(y_checked.sem, y_checked.before(b))
                    dve.tensor_scalar(abc[:, :, 1, :], bsm[:, 2, :, :], 10.0, -10.0, ALU.min, ALU.max)\
                       .then_inc(bb_s.sem, 1)
                    dve.wait_ge(bb_s.sem, bb_s.after(b, 1))
                    if follows(b):
                        dve.wait_ge(eb_mm.sem, eb_mm.before(b))
                    dve.scalar_tensor_tensor(bsm[:, 0, :, :], abc[:, :, 1, :], -1.0, abc[:, :, 1, :],
                                             ALU.mult, ALU.max).then_inc(bb_s.sem, 1)
                if slot in TURN_SLOTS:
                    c = TURN_SLOTS.index(slot)
                    if c == 0:
                        if follows(b):
                            dve.wait_ge(p_mm.sem, p_mm.before(b))
                    ln_lo_part(1, b, c, M1B[c])
                elif slot in X_SLOTS:
                    n = X_SLOTS.index(slot)
                    src = (A, B)[n % 2]
                    v = vpre[:, n % 2, :]
                    dve.wait_ge(conv0.sem, conv0.after(b, n))
                    for k in range(1, 4):
                        if k > 1:
                            dve.wait_ge(conv.sem, conv.after(b, 3 * n + k - 2))
                        dve.scalar_tensor_tensor(v[:, k:T], src[:, 0:T - k], cw[:, n, 3 - k:4 - k], v[:, k:T],
                                                 ALU.mult, ALU.add).then_inc(conv.sem, 1)
                if slot - 1 in X_SLOTS:
                    n = X_SLOTS.index(slot - 1)
                    dve.wait_ge(tanh_s.sem, tanh_s.after(b, n))
                    if n == 0:
                        if follows(b, 2):
                            dve.wait_ge(yy_s.sem, yy_s.after(b - 2, NC - 1))
                            dve.wait_ge(xt_tr.sem, xt_tr.after(b - 2, NC - 1))
                    dve.scalar_tensor_tensor(X[:, n, :], th[:, :], 1.0, vpre[:, n % 2, :], ALU.add, ALU.mult)\
                       .then_inc(xc_s.sem, 1)
                    dve.wait_ge(xc_s.sem, xc_s.after(b, n))
                    dve.tensor_reduce(xmax[:, par, n:n + 1], X[:, n, :], AX, ALU.max).then_inc(xmax_s.sem, 1)
                elif slot in Z_SLOTS:
                    n = Z_SLOTS.index(slot)
                    src = (B, A)[n % 2]
                    dve.wait_ge(tanh_s.sem, tanh_s.after(b, NC + n))
                    dve.scalar_tensor_tensor(sz[:, n, :], th[:, :], 1.0, src[:, :], ALU.add, ALU.mult)\
                       .then_inc(sz_s.sem, 1)

            def m2(b, par, slot):
                A, B = M2B
                X = xc[par]
                if slot == SUM_SLOT:
                    dve.wait_ge(eb_act.sem, eb_act.after(b, 0))
                    dve.tensor_tensor(bsm[:, 1, :, :], bsm[:, 1, :, :], abc[:, :, 1, :], ALU.mult).then_inc(bt_s.sem, 1)
                    dve.wait_ge(l_mm.sem, l_mm.after(b, 0))
                    dve.tensor_copy(lend[:, :, :], A[:, :].rearrange("p (k v w) -> p k v w", k=NT, v=NW)[:, :, :, W - 1])\
                       .then_inc(lend_s.sem, 1)
                    dve.wait_ge(bt_s.sem, bt_s.after(b, 0))
                    if follows(b):
                        dve.wait_ge(bT_tr.sem, bT_tr.before(b))
                    for j in range(NT):
                        ins = dve.tensor_tensor(bexp[:, j, :, :],
                                                bsm[:, 1, j, :].unsqueeze(1).to_broadcast([P, R8, S]),
                                                umask[:, j, :].unsqueeze(2).to_broadcast([P, R8, S]), ALU.mult)
                    ins.then_inc(bt_s.sem, 1)
                    dve.wait_ge(lend_s.sem, lend_s.after(b, 0))
                    dve.tensor_tensor(lbt[:, :, :],
                                      lend[:, :, :].rearrange("p k v -> p (k v)").unsqueeze(1)
                                      .to_broadcast([P, 2 * NT, NT * NW]), ends, ALU.mult).then_inc(lend_s.sem, 1)
                    dve.wait_ge(lend_s.sem, lend_s.after(b, 1))
                    dve.tensor_reduce(lbias[:, :], lbt[:, :, :], AX, ALU.add).then_inc(lend_s.sem, 1)
                    dve.wait_ge(lend_s.sem, lend_s.after(b, 2))
                    if follows(b):
                        dve.wait_ge(cf_s.sem, cf_s.before(b))
                    for h in range(2):
                        for i in (2 * h, 2 * h + 1):
                            o = EXO[h] + P * (i - 2 * h)
                            dve.tensor_scalar(ex[:, o:o + P], A[:, i * P:(i + 1) * P],
                                              lbias[:, h * NT + i:h * NT + i + 1], RANGE_SAFE,
                                              ALU.add, ALU.min).then_inc(lend_s.sem, 1)
                elif slot == CF_SLOT:
                    dve.wait_ge(c_tr.sem, c_tr.after(b, 0))
                    if follows(b):
                        dve.wait_ge(m_mm.sem, m_mm.before(b))
                    for h in range(2):
                        dve.wait_ge(lex_s.sem, lex_s.after(b, 2 + h))
                        n = T - 2 * P * h
                        dve.tensor_tensor(cf[:, EXO[h]:EXO[h] + n], ex[:, EXO[h]:EXO[h] + n],
                                          B[:, 2 * P * h:T], ALU.mult).then_inc(cf_s.sem, 1)
                elif slot == M_SLOTS[0]:
                    inc = lambda ins: ins.then_inc(bound_s.sem, 1)
                    dve.wait_ge(eb_act.sem, eb_act.after(b, 3))
                    inc(dve.tensor_tensor_scan(gsum[:, 3, :], gsum[:, 1, :], gsum[:, 0, :], 0.0, ALU.mult, ALU.add))
                    if follows(b):
                        dve.wait_ge(bound_tr.sem, bound_tr.before(b))
                    inc(dve.tensor_reduce(bound[0:S, 1:2], gsum[:, 2, :], AX, ALU.min))
                    dve.wait_ge(xmax_s.sem, xmax_s.after(b, NC - 1))
                    inc(dve.tensor_reduce(bound[:, 2:3], xmax[:, par, :], AX, ALU.max))
                    dve.wait_ge(bound_s.sem, bound_s.after(b, 0))
                    inc(dve.tensor_reduce(bound[0:S, 0:1], gsum[:, 3, :], AX, ALU.max))
                    dve.wait_ge(bound_s.sem, bound_s.after(b, 1))
                    inc(dve.tensor_scalar(bound[0:S, 1:2], bound[0:S, 1:2], -1.0, None, ALU.mult))
                    dve.wait_ge(bound_s.sem, bound_s.after(b, 2))
                    inc(dve.tensor_scalar(bound[:, 2:3], bound[:, 2:3], 0.56, None, ALU.max))
                    dve.wait_ge(bound_s.sem, bound_s.after(b, 5))
                    inc(dve.tensor_copy(bok[:, 0:1], bound[0:1, 2:3]))
                elif slot == BOUND_SLOT:
                    dve.wait_ge(bound_tr.sem, bound_tr.after(b, 0))
                    dve.tensor_reduce(brow[:, 0:3], B[0:1, 0:3 * P].rearrange("p (k n) -> p k n", k=3), AX, ALU.max)\
                       .then_inc(ok_s.sem, 1)
                    dve.wait_ge(ok_s.sem, ok_s.after(b, 0))
                    dve.tensor_tensor(bok[:, 1:2], brow[:, 0:1], brow[:, 2:3], ALU.mult).then_inc(ok_s.sem, 1)
                    dve.tensor_scalar(bok[:, 2:3], brow[:, 1:2], RANGE_SAFE, None, ALU.is_le).then_inc(ok_s.sem, 1)
                    dve.wait_ge(ok_s.sem, ok_s.after(b, 2))
                    if follows(b):
                        dve.wait_ge(y_checked.sem, y_checked.before(b))
                    dve.scalar_tensor_tensor(oki[:, :], bok[:, 1:2], H_SAFE2, bok[:, 2:3], ALU.is_le, ALU.mult)\
                       .then_inc(ok_s.sem, 1)
                elif slot in Y_SLOTS:
                    c = Y_SLOTS.index(slot)
                    dve.wait_ge(y_mm.sem, y_mm.after(b, c))
                    if c < 2:
                        if follows(b):
                            dve.wait_ge(yy_s.sem, yy_s.before(b))
                    else:
                        dve.wait_ge(yy_s.sem, yy_s.after(b, c - 2))
                    dve.tensor_tensor(t1[:, c % 2, :], (A, B)[c % 2][:, :], sz[:, c, :], ALU.mult).then_inc(t1_s.sem, 1)
                    dve.wait_ge(t1_s.sem, t1_s.after(b, c))
                    dve.wait_ge(y_checked.sem, y_checked.after(b, c))
                    if c == 0:
                        if follows(b):
                            dve.wait_ge(o_mm.sem, o_mm.before(b))
                    dve.scalar_tensor_tensor(yy[:, c, :], X[:, c, :], d2[:, c:c + 1], t1[:, c % 2, :],
                                             ALU.mult, ALU.add).then_inc(yy_s.sem, 1)
                elif slot in O_SLOTS:
                    o = O_SLOTS.index(slot)
                    dve.wait_ge(o_mm.sem, o_mm.after(b, o))
                    dve.wait_ge(x1_kept[o].sem, x1_kept[o].after(b, 15))
                    if follows(b):
                        dve.wait_ge(e_dve[1].sem, e_dve[1].after(b - 1, 4 * (2 * o + 1)))
                    two = slice(2 * o, 2 * o + 2)
                    dve.tensor_tensor(x2[:, two, :], (A, B)[o][:, :].rearrange("p (i d) -> p i d", i=2),
                                      x1m[:, two, :], ALU.add).then_inc(x2_s.sem, 1)

            def norms(it, par, on, slot):
                for l, (stage, b, p) in enumerate((("R1", it + 1, 0), ("F1", it, par), ("M2", it - 2, 0))):
                    if stage in on:
                        for i in range(NT):
                            if slot == LN_STAT[l][i]:
                                ln_stats(l, b, p, i)
                        if slot == LN_STAT[l][-1]:
                            ln_moments(l, b)
                        if slot == LN_APPLY[l] and l != 1:
                            ln_apply(l, b, p)
                if "M1" in on and slot == LN_APPLY[1]:
                    ln_apply(1, it - 1, (par + 1) % 2)

            def emit(it, par, on):
                for slot in range(SLOTS):
                    norms(it, par, on, slot)
                    for step in F1_STEPS.get(slot, ()) if "F1" in on else ():
                        moe(0, it, par, step)
                    for step in R1_STEPS.get(slot, ()) if "R1" in on else ():
                        moe(0, it + 1, par, step)
                    if "M2" in on:
                        m2(it - 2, par, slot)
                    for step in F2_STEPS.get(slot, ()) if "F2" in on else ():
                        moe(1, it - 3, (par + 1) % 2, step)
                    if "M1" in on:
                        m1(it - 1, (par + 1) % 2, slot)
            run(dve, emit)

        @block.gpsimd
        def _(pool):
            pool.memset(mhalf[:, :], -0.5).then_inc(s_pconst, 1)
            pool.wait_ge(s_pconst, 1)
            okreg = pool.alloc_register("y_ok")
            moved = pool.alloc_register("slow_dma_count")
            pool.reg_mov(moved, 0)

            def rstd(l, b):
                pool.wait_ge(ln_stat[l].sem, ln_stat[l].after(b, 2 * NT - 1))
                if follows(b):
                    pool.wait_ge(ln_xn[l].sem, ln_xn[l].before(b))
                apart(pool)
                pool.tensor_scalar(rs[l][:, 0, :], mv[l][:, :, 1], EPS, None, ALU.add).then_inc(ln_rstd[l].sem, 1)
                pool.wait_ge(ln_rstd[l].sem, ln_rstd[l].after(b, 0))
                pool.tensor_tensor(rs[l][:, 1, :], rs[l][:, 0, :], mhalf[:, :], ALU.pow).then_inc(ln_rstd[l].sem, 1)

            def moe(f, b, par, slot):
                X = x1[par] if f == 0 else x3
                if slot < 4 or slot % 2 == 0:
                    return
                g = slot - 4
                i, p = divmod(g, 4)
                tmp = etmp[f][:, (g // 2) % 2]
                pool.wait_ge(e_act[f].sem, e_act[f].after(b, g))
                if p == 1:
                    if i == 0:
                        if follows(b):
                            pool.wait_ge(e_pool[f].sem, e_pool[f].before(b))
                    else:
                        pool.wait_ge(e_pool[f].sem, e_pool[f].after(b, 4 * i - 1))
                    pool.tensor_tensor(esum[f][:, :], tmp[:, 0, :], tmp[:, 1, :], ALU.add).then_inc(e_pool[f].sem, 1)
                else:
                    for q in range(2):
                        pool.wait_ge(e_pool[f].sem, e_pool[f].after(b, 4 * i + q))
                        pool.tensor_tensor(esum[f][:, :], esum[f][:, :], tmp[:, q, :], ALU.add)\
                            .then_inc(e_pool[f].sem, 1)
                    pool.wait_ge(e_pool[f].sem, e_pool[f].after(b, 4 * i + 2))
                    pool.wait_ge(e_dve[f].sem, e_dve[f].after(b, 4 * i + 3))
                    pool.tensor_tensor(X[:, i, :], X[:, i, :], esum[f][:, :], ALU.add).then_inc(e_pool[f].sem, 1)

            def stepwise(b, par):
                X = xc[par]
                n = [0]

                def step(ins):
                    n[0] += 1
                    ins.then_inc(slow, 1)
                    pool.wait_ge(slow, n[0])

                pool.sem_clear(slow)
                done = pool.snap(moved)
                pool.wait_ge(a_exp.sem, a_exp.after(b, 0))
                pool.wait_ge(bb_s.sem, bb_s.after(b, 1))
                if follows(b):
                    pool.wait_ge(o_mm.sem, o_mm.before(b))
                if follows(b):
                    pool.wait_ge(yy_s.sem, yy_s.before(b))
                apart(pool)
                h, tmp, hc = (hst[:, k] for k in range(3))
                step(pool.memset(h, 0.0))
                step(pool.tensor_copy(abc[:, :, 2, :], td[:, :, S:2 * S]))
                pool.dma_start(scratch.ap().rearrange("(j p) r -> p j r", p=P),
                               abc[:, :, :, :].rearrange("p j k s -> p j (k s)")).then_inc(slow_dma, 16)
                pool.wait_ge(slow_dma, done + 16)
                apart(pool)
                G = bcast.shape[1]
                with pool.Fori(0, T // G) as g:
                    pool.dma_start(bcast[:, :, :, :].rearrange("p t k s -> p (t k s)"),
                                   scratch.ap()[bass.ds(g * G, G), :].rearrange("t r -> (t r)").unsqueeze(0)
                                   .to_broadcast([P, G * 3 * S])).then_inc(slow_dma, 16)
                    pool.wait_ge(slow_dma, done + (g + 2) * 16)
                    apart(pool)
                    pool.sem_clear(slow)
                    n[0] = 0
                    for t in range(G):
                        row = lambda k: bcast[:, t, k, :].unsqueeze(1).to_broadcast([P, NC, S])
                        xcol = X[:, :, bass.ds(g * G + t, 1)].to_broadcast([P, NC, S])
                        step(pool.tensor_tensor(h, h, row(0), ALU.mult))
                        step(pool.tensor_tensor(tmp, row(1), xcol, ALU.mult))
                        step(pool.tensor_tensor(h, h, tmp, ALU.add))
                        step(pool.tensor_scalar(h, h, H_LIMIT2, -H_LIMIT2, ALU.min, ALU.max))
                        step(pool.tensor_tensor(hc, h, row(2), ALU.mult))
                        w = S // 2
                        while w > 1:
                            step(pool.tensor_tensor(hc[:, :, 0:w], hc[:, :, 0:w], hc[:, :, w:2 * w], ALU.add))
                            w //= 2
                        step(pool.tensor_tensor(yy[:, :, bass.ds(g * G + t, 1)], hc[:, :, 0:1], hc[:, :, 1:2], ALU.add))

                pool.reg_add(moved, moved, 16 * (1 + T // G))

            def m1(b, slot):
                if slot == DT_SLOT:
                    pool.wait_ge(td_s.sem, td_s.after(b, 0))
                    if follows(b):
                        pool.wait_ge(c_tr.sem, c_tr.before(b))
                    apart(pool)
                    pool.tensor_copy(crep[:, :, :, :], td[:, :, S:2 * S].unsqueeze(2).to_broadcast([P, NT, R8, S]))\
                        .then_inc(crep_s.sem, 1)

            def m2(b, par, slot):
                if slot in M_SLOTS:
                    j = M_SLOTS.index(slot)
                    pool.wait_ge(m_act.sem, m_act.after(b, j))
                    pool.tensor_tensor(mt[j][:, 0:P], mt[j][:, 0:P], tri, ALU.mult).then_inc(m_tri.sem, 1)
                elif slot == BOUND_SLOT:
                    pool.wait_ge(ok_s.sem, ok_s.after(b, 3))
                    apart(pool)
                    pool.reg_load(okreg, oki[0:1, 0:1])
                    with pool.If_eq(okreg, 0):
                        stepwise(b, par)
                if slot in XT_SLOTS:
                    c = XT_SLOTS.index(slot)
                    with pool.If_eq(okreg, 0):
                        pool.wait_ge(t1_s.sem, t1_s.after(b, c))
                        apart(pool)
                        pool.sem_clear(slow)
                        pool.tensor_tensor(t1[:, c % 2, :], yy[:, c, :], sz[:, c, :], ALU.mult).then_inc(slow, 1)
                        pool.wait_ge(slow, 1)
                    pool.sem_inc(y_checked.sem, 1)

            def emit(it, par, on):
                for slot in range(SLOTS):
                    for l, (stage, b) in enumerate((("R1", it + 1), ("F1", it), ("M2", it - 2))):
                        if stage in on and slot == LN_STAT[l][-1]:
                            rstd(l, b)
                    for step in F1_STEPS.get(slot, ()) if "F1" in on else ():
                        moe(0, it, par, step)
                    if "M2" in on:
                        m2(it - 2, par, slot)
                    for step in F2_STEPS.get(slot, ()) if "F2" in on else ():
                        moe(1, it - 3, (par + 1) % 2, step)
                    if "M1" in on:
                        m1(it - 1, slot)
            run(pool, emit)


def kernel(L0_attn_x, L0_attn_W_in, L0_attn_conv_w, L0_attn_conv_b, L0_attn_W_xproj, L0_attn_A_log,
           L0_attn_D_param, L0_attn_W_out, L0_ffn_gate_w, L0_ffn_expert_w):
    import concourse.bacc as bacc
    from concourse.bass_utils import run_bass_kernel_spmd

    def chunks(a):
        return np.ascontiguousarray(a.reshape(-1, P, a.shape[-1]).transpose(1, 0, 2))

    def column(a):
        return np.ascontiguousarray(a.reshape(NC, P).T)

    x = np.asarray(L0_attn_x)
    ew = np.asarray(L0_ffn_expert_w)
    arrays = {
        "x": np.ascontiguousarray(x.reshape(NB * T, D)),
        "w_exp": chunks(ew.transpose(2, 0, 1).reshape(D, NE * D)),
        "w_gate": chunks(np.asarray(L0_ffn_gate_w).T),
        "w_in": chunks(np.asarray(L0_attn_W_in).T),
        "w_xd": chunks(np.asarray(L0_attn_W_xproj).T),
        "w_out": chunks(np.asarray(L0_attn_W_out).T),
        "conv_w": chunks(np.asarray(L0_attn_conv_w)),
        "conv_b": column(np.asarray(L0_attn_conv_b)),
        "d_par": column(np.asarray(L0_attn_D_param)),
        "a_log": np.ascontiguousarray(np.broadcast_to(np.asarray(L0_attn_A_log), (P, S))),
        "consts": constants(),
    }
    nc = bacc.Bacc("TRN2", target_bir_lowering=False, num_devices=1)
    aps = [nc.dram_tensor(n, a.shape, F32, kind="ExternalInput").ap() for n, a in arrays.items()]
    out = nc.dram_tensor("out", (NB * T, D), F32, kind="ExternalOutput").ap()
    build(nc, *aps, out)
    r = run_bass_kernel_spmd(nc, [arrays], core_ids=[0])
    return r.results[0]["out"].reshape(x.shape)
```
